# Optimizing a Trainium2 kernel written in Bass

```python
import numpy as np
import jax
import jax.numpy as jnp

def _softmax(x, axis=-1):
    return jax.nn.softmax(x, axis=axis)
def _gelu(x):
    return jax.nn.gelu(x, approximate=True)
def _silu(x):
    return jax.nn.silu(x)
def _sigmoid(x):
    return jax.nn.sigmoid(x)
def _layernorm(x, axis=-1, eps=1e-5):
    m = jnp.mean(x, axis=axis, keepdims=True)
    v = jnp.var(x, axis=axis, keepdims=True)
    return (x - m) / jnp.sqrt(v + eps)
def _scatter_add(tgt, idx, src, axis=0):
    return tgt.at[idx].add(src)
def _segment_sum(src, seg, n):
    return jax.ops.segment_sum(src, seg, n)

kernel_name = 'mk_conv_preact_d1_conv_nchw16_b038a4'

def setup_inputs(seed: int = 0):
    np.random.seed(seed)
    _w = jnp.asarray
    def _rec_inputs():
        import jax
        import jax.numpy as jnp
        _gk = jax.random.key(seed)
        x = -7.109e-05 + 0.9999 * jax.random.normal(jax.random.fold_in(_gk, 1), (16, 16, 512, 512), jnp.float32)
        return x
    x = _rec_inputs()
    def _L0_conv_setup():
        import jax, jax.numpy as jnp
        import numpy as np
        B, C_IN, H, W = (16, 16, 512, 512)
        C_OUT, KH, KW = (16, 3, 3)
        N_EXPERTS = 3
        key = jax.random.key(seed)
        k1, k2, k3, k4 = jax.random.split(key, 4)
        x = jax.random.normal(k1, (B, C_IN, H, W), dtype=jnp.float32)
        fan_in = C_IN * KH * KW
        bound = np.sqrt(6.0 / fan_in)
        w_experts = jax.random.uniform(k2, (N_EXPERTS, C_OUT, C_IN, KH, KW), minval=-bound, maxval=bound, dtype=jnp.float32)
        bias = jnp.zeros((C_OUT,), dtype=jnp.float32)
        fc_bound = 1.0 / np.sqrt(C_IN)
        fc_w = jax.random.uniform(k3, (N_EXPERTS, C_IN), minval=-fc_bound, maxval=fc_bound, dtype=jnp.float32)
        fc_b = jnp.zeros((N_EXPERTS,), dtype=jnp.float32)
        return {'x': x, 'w_experts': w_experts, 'bias': bias, 'fc_w': fc_w, 'fc_b': fc_b}
    _L0_conv_all = _L0_conv_setup()
    _L0_conv_in = {k: v for k, v in _L0_conv_all.items() if k in ('w_experts', 'bias', 'fc_w', 'fc_b', )}
    del _L0_conv_all

    return {
        "x": x,
        "L0_conv_w_experts": _L0_conv_in["w_experts"],
        "L0_conv_bias": _L0_conv_in["bias"],
        "L0_conv_fc_w": _L0_conv_in["fc_w"],
        "L0_conv_fc_b": _L0_conv_in["fc_b"],
    }

def reference(x, L0_conv_w_experts, L0_conv_bias, L0_conv_fc_w, L0_conv_fc_b):
    import jax
    import jax.numpy as jnp
    def _L0_conv_ref(x, w_experts, bias, fc_w, fc_b):
        import jax, jax.numpy as jnp
        import numpy as np
        B, C_IN, H, W = (16, 16, 512, 512)
        C_OUT, KH, KW = (16, 3, 3)
        N_EXPERTS = 3
        pooled = x.mean(axis=(2, 3))
        routing = jax.nn.softmax(pooled @ fc_w.T + fc_b, axis=1)
        kernels = jnp.einsum('bn,noihw->boihw', routing, w_experts)
        xp = jnp.pad(x, ((0, 0), (0, 0), (1, 1), (1, 1)), mode='reflect')

        def conv_one(xi, ki):
            return jax.lax.conv_general_dilated(xi[None], ki, window_strides=(1, 1), padding='VALID', dimension_numbers=('NCHW', 'OIHW', 'NCHW'))[0]
        out = jax.vmap(conv_one)(xp, kernels)
        return out + bias[None, :, None, None]

    def _gn(v, G=8, eps=1e-5):
        B_, C_, H_, W_ = v.shape
        g = v.reshape(B_, G, C_ // G, H_, W_)
        m = jnp.mean(g, axis=(2, 3, 4), keepdims=True)
        s = jnp.var(g, axis=(2, 3, 4), keepdims=True)
        return ((g - m) / jnp.sqrt(s + eps)).reshape(v.shape)

    def _ln_c(v, eps=1e-6):
        m = jnp.mean(v, axis=1, keepdims=True)
        s = jnp.var(v, axis=1, keepdims=True)
        return (v - m) / jnp.sqrt(s + eps)

    def _ln_t(v, eps=1e-5):
        m = jnp.mean(v, axis=-1, keepdims=True)
        s = jnp.var(v, axis=-1, keepdims=True)
        return (v - m) / jnp.sqrt(s + eps)

    def _to_tokens(v):
        B_, C_, H_, W_ = v.shape
        return v.reshape(B_, C_, H_ * W_).transpose(0, 2, 1)
    def _from_tokens(t, like):
        B_, C_, H_, W_ = like.shape
        return t.transpose(0, 2, 1).reshape(B_, C_, H_, W_)

    x = x + _L0_conv_ref(_gn(x), L0_conv_w_experts, L0_conv_bias, L0_conv_fc_w, L0_conv_fc_b)
    return x


_drawn_inputs = setup_inputs


def setup_inputs(seed=0):
    import zlib

    import numpy as np

    out = dict(_drawn_inputs(seed))
    spreads = {'L0_conv_bias': (0.0, 0.1), 'L0_conv_fc_b': (0.0, 0.299)}
    factors = {'L0_conv_fc_w': 172.409}
    for name, (base, spread) in spreads.items():
        noise = np.random.default_rng([zlib.crc32(name.encode()), seed]).standard_normal(out[name].shape)
        drawn = base * np.exp(spread * noise) if base else spread * noise
        out[name] = jnp.asarray(drawn.astype(out[name].dtype))
    for name, factor in factors.items():
        out[name] = (out[name] * factor).astype(out[name].dtype)
    return out
```

```python
from contextlib import ExitStack

import concourse.bass as bass
from concourse import mybir

F32 = mybir.dt.float32
F32R = mybir.dt.float32r
ALU = mybir.AluOpType
ACT = mybir.ActivationFunctionType
AX_X = mybir.AxisListType.X

P = 128
EPS = 1e-5
ROWS = 8
STEP = ROWS - 2
GROUP = 5
RING_GROUPS = 19
LAG = 2
STATS = 6
KW = 3


def conv_kernel(nc, x, expert_rows, bias, fc_wT, fc_b, share, sums_w, identity, out):
    B, C, H, W = x.shape
    E = fc_wT.shape[1]
    TILES = (H - 2) // STEP
    GROUPS = TILES // GROUP
    ALL_GROUPS = B * GROUPS
    INNER = STEP * C
    EARLY = TILES - GROUP
    assert C * ROWS == P and TILES * STEP + 2 == H and GROUPS * GROUP == TILES and GROUPS + 2 == RING_GROUPS
    assert 2 * KW * P <= W * 2 and 0 < LAG < GROUP

    with ExitStack() as ctx:
        def sb(name, shape, dt=F32):
            return ctx.enter_context(nc.sbuf_tensor(name, shape, dt))

        def sem(name):
            return ctx.enter_context(nc.semaphore(name))

        tiles = sb("tiles", [P, RING_GROUPS * GROUP * W])
        x_hi = sb("x_hi", [P, GROUP, W + 2], F32R)
        x_lo = sb("x_lo", [P, GROUP, W + 2], F32R)
        bands = sb("bands", [P, E, KW, P])
        w_hi = sb("w_hi", [P, KW, P], F32R)
        w_lo = sb("w_lo", [P, KW, P], F32R)
        centre = sb("centre", [P, P])
        sums_sb = sb("sums_sb", [P, 3, P])
        ones = sb("ones", [P, P])
        stats = sb("stats", [P, TILES, STATS])
        share_sb = sb("share_sb", [P, 3, 2])
        fc_w_sb = sb("fc_w_sb", [P, E])
        fc_b_sb = sb("fc_b_sb", [1, E])
        bias_sb = sb("bias_sb", [P, 1])
        numbers = sb("numbers", [P, 72 + B])
        taken = [0]

        def few(count, parts=1):
            start = taken[0]
            taken[0] += count * parts
            assert taken[0] <= 72 + B
            view = numbers[:, start:taken[0]]
            return view if parts == 1 else view.rearrange("p (a b) -> p a b", b=parts)

        mean_var = few(3, 2)
        shared = few(3, 2)
        means = few(2)
        neg_mean = few(1)
        mean_bias = few(1)
        out_bias = few(B)
        deviation = few(3)
        share_dev = few(3)
        spread = few(3)
        var_eps = few(1)
        minus_half = few(1)
        rstd = few(1)
        fc_in = few(E)
        logit_max = few(1)
        logits = few(E)
        expd = few(E)
        exp_sum = few(1)
        inv_sum = few(1)
        mix = few(E)

        acc = ctx.enter_context(nc.psum_tensor("acc", [P, GROUP, W], F32))
        small = ctx.enter_context(nc.psum_tensor("small", [P, 3, W], F32))
        both_means, group_mean, channel_off = small[:, 0, 0:2], small[:, 0, 0:1], small[:, 0, 1:2]
        bias_sum, variance, logit_sum = small[:, 0, 2:3], small[:, 1, 0:1], small[:, 2, 0:E]
        w_full = small[:, 1, P:P + KW * P].rearrange("p (k m) -> p k m", k=KW)

        PARTS = ROWS + 2
        last_slots = (RING_GROUPS * GROUP - LAG) * W
        row_flat = tiles[:, last_slots - PARTS * E * KW * C:last_slots]
        row_parts = row_flat.rearrange("p (j k c) -> p j k c", j=PARTS, c=C)
        SPARE = GROUP - LAG
        assert PARTS * E * KW * C <= SPARE * W

        x_loaded = [sem(f"x_loaded{i}") for i in range(GROUP)]
        y_stored = [sem(f"y_stored{i}") for i in range(GROUP)]
        top_stored = sem("top_stored")
        bottom_stored = sem("bottom_stored")
        const_loaded = sem("const_loaded")
        rows_loaded = sem("rows_loaded")
        zeroed = sem("zeroed")
        setup_done = sem("setup_done")
        dve_step = sem("dve_step")
        stats_done = sem("stats_done")
        aggregated = sem("aggregated")
        shared_ready = sem("shared_ready")
        means_ready = sem("means_ready")
        centred = sem("centred")
        mean_bias_ready = sem("mean_bias_ready")
        spread_ready = sem("spread_ready")
        variance_ready = sem("variance_ready")
        var_eps_ready = sem("var_eps_ready")
        rstd_ready = sem("rstd_ready")
        fc_in_ready = sem("fc_in_ready")
        bias_summed = sem("bias_summed")
        out_bias_ready = sem("out_bias_ready")
        logits_summed = sem("logits_summed")
        logits_ready = sem("logits_ready")
        exp_ready = sem("exp_ready")
        weights_ready = sem("weights_ready")
        hi_ready = sem("hi_ready")
        lo_ready = sem("lo_ready")
        conv_done = sem("conv_done")
        y_ready = sem("y_ready")

        held_before = [0]

        def held(eng, name, value, most):
            held_before[0] += 1
            register = eng.alloc_register(f"{name}{held_before[0]}")
            eng.reg_mov(register, value)
            return eng.snap(register, donate=True, min_val=0, max_val=most)

        def ring_start(eng, g, name="ring_at"):
            return held(eng, name, (g % RING_GROUPS) * (GROUP * W), (RING_GROUPS - 1) * GROUP * W)

        def slot(start, i):
            return tiles[:, bass.ds(start + i * W, W)]

        def dram_rows(t, row, count):
            whole = bass.AP(tensor=t.tensor, offset=0, ap=[[H * W, C], [1, (B - 1) * C * H * W + H * W]])
            return whole[:, bass.ds(row * W, count * W)]

        block = ctx.enter_context(nc.Block())

        @block.sync
        def _(sp):
            def first_row(g, name):
                return held(sp, name, (g // GROUPS) * (C * H) + (g % GROUPS) * (GROUP * STEP),
                            (B - 1) * C * H + (GROUPS - 1) * GROUP * STEP)

            def load(at, src, i):
                sp.dma_start(slot(at, i), dram_rows(x, src + i * STEP, ROWS)).then_inc(x_loaded[i], 16)

            def store(g, at, dst, i):
                sp.wait_ge(y_ready, g * GROUP + i + 1)
                sp.dma_start(dram_rows(out, dst + (i * STEP + 1), STEP), slot(at, i)[0:INNER, :]
                             ).then_inc(y_stored[i], 16)

            def counts(g):
                most = 16 * ALL_GROUPS
                return (held(sp, "stored_count", (g - RING_GROUPS + 1) * 16, most),
                        held(sp, "tops_count", ((g - RING_GROUPS) // GROUPS + 1) * 16, most),
                        held(sp, "bottoms_count", ((g - RING_GROUPS + 1) // GROUPS) * 16, most),
                        held(sp, "loaded_count", g * 16, most))

            def refill(at, src, i, reached):
                stored, tops, bottoms, loaded = reached
                sp.wait_ge(y_stored[i], stored)
                if i == 0:
                    sp.wait_ge(top_stored, tops)
                if i == GROUP - 1:
                    sp.wait_ge(bottom_stored, bottoms)
                sp.wait_ge(x_loaded[i], loaded)
                load(at, src, i)

            def turn(g, before=True, here=True):
                at, dst = ring_start(sp, g), first_row(g, "store_at")
                if before:
                    at_before = ring_start(sp, g + RING_GROUPS - 1, "ring_before")
                    src_before = first_row(g + RING_GROUPS - 1, "load_before")
                    reached_before = counts(g + RING_GROUPS - 1)
                if here:
                    src = first_row(g + RING_GROUPS, "load_at")
                    reached = counts(g + RING_GROUPS)
                for i in range(GROUP):
                    store(g, at, dst, i)
                    if i < LAG and before:
                        refill(at_before, src_before, i + GROUP - LAG, reached_before)
                    if i >= LAG and here:
                        refill(at, src, i - LAG, reached)

            for i in range(GROUP):
                load(0, 0, i)
            with sp.Fori(1, RING_GROUPS - 1) as g:
                at, src = ring_start(sp, g), first_row(g, "load_at")
                for i in range(GROUP):
                    sp.wait_ge(x_loaded[i], 16 * g)
                    load(at, src, i)
            sp.wait_ge(setup_done, 1)
            last = RING_GROUPS - 1
            for i in range(GROUP - LAG):
                sp.wait_ge(x_loaded[i], 16 * last)
                load(last * GROUP * W, (last // GROUPS) * C * H + (last % GROUPS) * GROUP * STEP, i)

            with sp.Fori(0, ALL_GROUPS - RING_GROUPS) as g:
                turn(g)
            turn(ALL_GROUPS - RING_GROUPS, here=False)
            with sp.Fori(ALL_GROUPS - RING_GROUPS + 1, ALL_GROUPS) as g:
                turn(g, before=False, here=False)
            for i in range(GROUP):
                sp.wait_ge(y_stored[i], 16 * ALL_GROUPS)
            sp.wait_ge(top_stored, 16 * B)
            sp.wait_ge(bottom_stored, 16 * B)

        @block.gpsimd
        def _(pool):
            pool.dma_start(sums_sb[:], sums_w).then_inc(const_loaded, 16)
            pool.dma_start(centre[:], identity).then_inc(const_loaded, 16)
            pool.dma_start(share_sb[:], share).then_inc(const_loaded, 16)
            pool.dma_start(fc_b_sb[:], fc_b).then_inc(const_loaded, 16)
            pool.wait_ge(zeroed, 3)
            pool.dma_start(bias_sb[0:P:ROWS, :], bias).then_inc(const_loaded, 16)
            pool.dma_start(fc_w_sb[0:P:ROWS, :], fc_wT).then_inc(const_loaded, 16)
            for j in range(ROWS):
                for kh in range(3):
                    r = j + kh - 1
                    if 0 <= r < ROWS:
                        pool.dma_start(row_parts[r:P:ROWS, j], expert_rows[kh]).then_inc(rows_loaded, 16)
            pool.dma_start(row_parts[1:P:ROWS, ROWS], expert_rows[0]).then_inc(rows_loaded, 16)
            pool.dma_start(row_parts[ROWS - 2:P:ROWS, ROWS + 1], expert_rows[2]).then_inc(rows_loaded, 16)

            def inverse_deviation(s):
                pool.wait_ge(var_eps_ready, s + 1)
                nc.gpsimd.tensor_tensor(rstd[:], var_eps[:], minus_half[:], ALU.pow).then_inc(rstd_ready, 1)

            def store_edge(s, t, row, partition, stored):
                at = held(pool, "ring_at", ((s * GROUPS + t // GROUP) % RING_GROUPS) * (GROUP * W),
                          (RING_GROUPS - 1) * GROUP * W)
                dst = held(pool, "store_at", s * (C * H), (B - 1) * C * H)
                pool.wait_ge(y_ready, s * TILES + t + 1)
                pool.dma_start(dram_rows(out, dst + row, 1),
                               slot(at, t % GROUP)[partition:partition + C, :]).then_inc(stored, 16)

            inverse_deviation(0)
            with pool.Fori(0, B - 1) as s:
                store_edge(s, 0, 0, INNER, top_stored)
                inverse_deviation(s + 1)
                store_edge(s, TILES - 1, H - 1, INNER + C, bottom_stored)
            store_edge(B - 1, 0, 0, INNER, top_stored)
            store_edge(B - 1, TILES - 1, H - 1, INNER + C, bottom_stored)

        @block.tensor
        def _(pe):
            def sum_means(s):
                pe.wait_ge(shared_ready, s + 1)
                for what, mean in ((0, group_mean), (1, channel_off)):
                    for k in range(3):
                        mm = pe.matmul(mean, sums_sb[:, what, :], shared[:, k, 0:1], start=k == 0, stop=k == 2)
                mm.then_inc(means_ready, 1)

            def sum_variance(s):
                pe.wait_ge(mean_bias_ready, s + 1)
                pe.matmul(bias_sum, sums_sb[:, 2, :], mean_bias[:], start=True, stop=True).then_inc(bias_summed, 1)
                for k in range(3):
                    pe.matmul(variance, sums_sb[:, 0, :], shared[:, k, 1:2], start=k == 0, stop=False)
                pe.wait_ge(spread_ready, s + 1)
                for k in range(3):
                    mm = pe.matmul(variance, sums_sb[:, 0, :], spread[:, k:k + 1], start=False, stop=k == 2)
                mm.then_inc(variance_ready, 1)

            def sum_logits(s):
                pe.wait_ge(fc_in_ready, s + 1)
                pe.matmul(logit_sum, ones[:, :], fc_in[:, :], start=True, stop=False)
                pe.matmul(logit_sum, ones[0:1, :], fc_b_sb[:, :], start=False, stop=True).then_inc(logits_summed, 1)

            def conv(s, j, i, fresh_banks=False, fresh_weights=False):
                n = (s * GROUPS + j) * GROUP + i
                pe.wait_ge(lo_ready, 2 * (n + 1))
                if not fresh_banks:
                    pe.wait_ge(y_ready, n - GROUP + 1)
                for k in range(KW):
                    if fresh_weights:
                        pe.wait_ge(weights_ready, s * KW + k + 1)
                    for w, part in ((w_hi, x_hi), (w_lo, x_hi), (w_hi, x_lo)):
                        mm = pe.matmul(acc[:, i, :], w[:, k, :], part[:, i, k:k + W],
                                       start=k == 0 and w is w_hi and part is x_hi,
                                       stop=k == KW - 1 and part is x_lo)
                mm.then_inc(conv_done, 1)

            def sample(s, first=False, last=False):
                for i in range(GROUP):
                    conv(s, 0, i, fresh_banks=first, fresh_weights=i == 0)
                with pe.Fori(1, GROUPS - 1) as j:
                    for i in range(GROUP):
                        conv(s, j, i)
                for i in range(GROUP):
                    conv(s, GROUPS - 1, i)
                    if not last and i < 3:
                        (sum_means, sum_variance, sum_logits)[i](s + 1)

            pe.wait_ge(setup_done, 1)
            sum_means(0)
            sum_variance(0)
            sum_logits(0)
            sample(0, first=True)
            with pe.Fori(1, B - 1) as s:
                sample(s)
            sample(B - 1, last=True)

        @block.scalar
        def _(act):
            def high(at, i):
                src = slot(at, i)
                act.activation(x_hi[:, i, 1:W + 1], src, ACT.Identity, bias=neg_mean[:, 0:1]).then_inc(hi_ready, 1)
                act.activation(x_hi[:, i, 0:W + 2:W + 1], src[:, 1:W - 1:W - 3], ACT.Identity,
                               bias=neg_mean[:, 0:1]).then_inc(hi_ready, 1)

            def result(s, j, at, i):
                act.wait_ge(conv_done, (s * GROUPS + j) * GROUP + i + 1)
                act.activation(slot(at, i), acc[:, i, :], ACT.Identity,
                               bias=out_bias[:, bass.ds(s, 1)]).then_inc(y_ready, 1)

            def exponentials(s):
                act.wait_ge(logits_ready, s + 1)
                act.activation(expd[:], logits[:], ACT.Exp, accum_out=exp_sum[:]).then_inc(exp_ready, 1)

            def inside(s):
                with act.Fori(1, GROUPS) as j:
                    before = ring_start(act, s * GROUPS + j - 1, "ring_before")
                    at = ring_start(act, s * GROUPS + j)
                    for i in range(GROUP):
                        result(s, j - 1, before, i)
                        high(at, i)

            act.wait_ge(centred, 1)
            for i in range(GROUP):
                high(0, i)
            exponentials(0)
            act.wait_ge(out_bias_ready, 1)
            with act.Fori(0, B - 1) as s:
                inside(s)
                before = ring_start(act, s * GROUPS + GROUPS - 1, "ring_before")
                at = ring_start(act, (s + 1) * GROUPS)
                for i in range(GROUP):
                    result(s, GROUPS - 1, before, i)
                    if i == 0:
                        act.wait_ge(centred, s + 2)
                    high(at, i)
                    if i == 2:
                        exponentials(s + 1)
                act.wait_ge(out_bias_ready, s + 2)
            inside(B - 1)
            before = ring_start(act, (B - 1) * GROUPS + GROUPS - 1, "ring_before")
            for i in range(GROUP):
                result(B - 1, GROUPS - 1, before, i)

        @block.vector
        def _(dve):
            SETUP = 2 + ROWS
            STEPS = 11
            done = [0]

            def link(ins, base=0):
                done[0] += 1
                ins.then_inc(dve_step, 1)
                dve.wait_ge(dve_step, base + done[0])

            def low(n, at, i):
                dve.wait_ge(hi_ready, 2 * (n + 1))
                src = slot(at, i)
                hi = x_hi[:, i, :].bitcast(F32)
                dve.scalar_tensor_tensor(x_lo[:, i, 1:W + 1], src, neg_mean[:, 0:1], hi[:, 1:W + 1],
                                         ALU.add, ALU.subtract).then_inc(lo_ready, 1)
                dve.scalar_tensor_tensor(x_lo[:, i, 0:W + 2:W + 1], src[:, 1:W - 1:W - 3], neg_mean[:, 0:1],
                                         hi[:, 0:W + 2:W + 1], ALU.add, ALU.subtract).then_inc(lo_ready, 1)

            def tile_stats(g, j, at, i):
                dve.wait_ge(x_loaded[i], 16 * (g + 1))
                dve.bn_stats(stats[:, bass.ds(j * GROUP + i, 1), :].rearrange("p o k -> p (o k)"),
                             slot(at, i)).then_inc(stats_done, 1)

            def routing(s):
                done[0] = 0
                base = STEPS * s + SETUP
                dve.wait_ge(stats_done, TILES * (s + 1))
                dve.memset(deviation[:], 0.0)
                dve.bn_aggr(mean_var[:, 0, :], stats[:, 0:EARLY, :]).then_inc(aggregated, 1)
                dve.bn_aggr(mean_var[:, 1, :], stats[:, EARLY:TILES, :]).then_inc(aggregated, 1)
                dve.bn_aggr(mean_var[:, 2, :], stats[:, TILES - 1, :]).then_inc(aggregated, 1)
                dve.wait_ge(aggregated, 3 * (s + 1))
                dve.tensor_tensor(shared[:], mean_var[:], share_sb[:], ALU.mult).then_inc(shared_ready, 1)
                dve.wait_ge(means_ready, s + 1)
                link(dve.tensor_copy(means[:], both_means), base)
                dve.tensor_tensor(mean_bias[:], bias_sb[:], means[:, 0:1], ALU.add).then_inc(mean_bias_ready, 1)
                dve.tensor_scalar(neg_mean[:], means[:, 0:1], -1.0, None, ALU.mult).then_inc(centred, 1)
                dve.scalar_tensor_tensor(share_dev[:], mean_var[:, :, 0], means[:, 0:1], share_sb[:, :, 0],
                                         ALU.subtract, ALU.mult)
                link(dve.tensor_scalar(deviation[:], mean_var[:, :, 0], means[:, 0:1], None, ALU.subtract), base)
                dve.tensor_tensor(spread[:], deviation[:], share_dev[:], ALU.mult).then_inc(spread_ready, 1)
                dve.wait_ge(variance_ready, s + 1)
                dve.tensor_scalar(var_eps[:], variance, EPS, None, ALU.add).then_inc(var_eps_ready, 1)
                dve.wait_ge(bias_summed, s + 1)
                dve.tensor_copy(out_bias[:, bass.ds(s, 1)], bias_sum).then_inc(out_bias_ready, 1)
                dve.wait_ge(rstd_ready, s + 1)
                dve.tensor_scalar(fc_in[:], fc_w_sb[:], means[:, 1:2], rstd[:, 0:1],
                                  ALU.mult, ALU.mult).then_inc(fc_in_ready, 1)
                dve.wait_ge(logits_summed, s + 1)
                link(dve.reduce_max(logit_max[:], logit_sum, AX_X), base)
                dve.tensor_scalar(logits[:], logit_sum, logit_max[:, 0:1], None, ALU.subtract).then_inc(logits_ready, 1)
                dve.wait_ge(exp_ready, s + 1)
                link(dve.reciprocal(inv_sum[:], exp_sum[:]), base)
                link(dve.tensor_scalar(mix[:], expd[:], inv_sum[:, 0:1], rstd[:, 0:1], ALU.mult, ALU.mult), base)
                dve.tensor_scalar(w_full[:, 0:KW:2], bands[:, 0, 0:KW:2], mix[:, 0:1], None, ALU.mult)
                link(dve.scalar_tensor_tensor(w_full[:, 1], bands[:, 0, 1], mix[:, 0:1], centre[:],
                                              ALU.mult, ALU.add), base)
                for e in range(1, E):
                    link(dve.scalar_tensor_tensor(w_full[:], bands[:, e], mix[:, e:e + 1], w_full[:],
                                                  ALU.mult, ALU.add), base)

            def weights(s):
                base = STEPS * s + SETUP
                if not isinstance(s, int) or s > 0:
                    dve.wait_ge(conv_done, s * TILES)
                for k in range(KW):
                    ins = dve.tensor_copy(w_hi[:, k], w_full[:, k])
                    done[0] += 1
                    ins.then_inc(dve_step, 1)
                for k in range(KW):
                    dve.wait_ge(dve_step, base + done[0] - KW + 1 + k)
                    dve.tensor_tensor(w_lo[:, k], w_full[:, k], w_hi[:, k].bitcast(F32),
                                      ALU.subtract).then_inc(weights_ready, 1)
                assert done[0] == STEPS, done

            def sample(s, ahead):
                with dve.Fori(1, GROUPS) as j:
                    g = s * GROUPS + j
                    at = ring_start(dve, g)
                    if ahead:
                        at_next = ring_start(dve, g + GROUPS, "ring_next")
                    for i in range(GROUP):
                        low(g * GROUP + i, at, i)
                        if ahead:
                            tile_stats(g + GROUPS, j, at_next, i)

            def first_turn(s, ahead=True):
                g = s * GROUPS
                at = ring_start(dve, g)
                if ahead:
                    at_next = ring_start(dve, g + GROUPS, "ring_next")
                for i in range(GROUP):
                    low(g * GROUP + i, at, i)
                    if i == 1:
                        weights(s)
                if ahead:
                    for i in range(GROUP):
                        tile_stats(g + GROUPS, 0, at_next, i)

            dve.memset(row_flat, 0.0).then_inc(zeroed, 1)
            dve.memset(bias_sb[:], 0.0).then_inc(zeroed, 1)
            dve.memset(fc_w_sb[:], 0.0).then_inc(zeroed, 1)
            link(dve.memset(ones[:], 1.0))
            link(dve.memset(minus_half[:], -0.5))
            dve.wait_ge(const_loaded, 16 * 6)
            dve.wait_ge(rows_loaded, 16 * 3 * ROWS)
            cols = bands[:].rearrange("p e k m -> p (e k) m")
            edge = {0: INNER, ROWS - 1: INNER + C}
            for j in range(ROWS):
                if j in edge:
                    link(dve.tensor_tensor(cols[:, :, edge[j]:edge[j] + C], row_parts[:, j],
                                           row_parts[:, ROWS + (j > 0)], ALU.add))
                else:
                    link(dve.tensor_copy(cols[:, :, j - 1:INNER:STEP], row_parts[:, j]))
            assert done[0] == SETUP
            dve.tensor_copy(inv_sum[:], minus_half[:]).then_inc(setup_done, 1)
            with dve.Fori(0, GROUPS) as g:
                at = ring_start(dve, g)
                for i in range(GROUP):
                    tile_stats(g, g, at, i)
            routing(0)
            first_turn(0)
            with dve.Fori(0, B - 2) as s:
                sample(s, True)
                routing(s + 1)
                first_turn(s + 1)
            sample(B - 2, True)
            routing(B - 1)
            first_turn(B - 1, ahead=False)
            sample(B - 1, False)


def kernel(x, L0_conv_w_experts, L0_conv_bias, L0_conv_fc_w, L0_conv_fc_b):
    import numpy as np
    import concourse.bacc as bacc
    from concourse.bass_utils import run_bass_kernel_spmd

    x = np.ascontiguousarray(x)
    B, C, H, W = x.shape
    E = L0_conv_w_experts.shape[0]
    expert_rows = np.ascontiguousarray(
        np.asarray(L0_conv_w_experts).transpose(3, 2, 0, 4, 1)).reshape(3, C, E * 3, C)

    inner = STEP * C
    c_in, r_in = np.arange(P)[:, None] // ROWS, np.arange(P)[:, None] % ROWS
    m = np.arange(P)[None, :]
    c_out = np.where(m < inner, m // STEP, (m - inner) % C)
    r_out = np.where(m < inner, m % STEP + 1, np.where(m < inner + C, 0, ROWS - 1))
    tiles = (H - 2) // STEP
    share = np.concatenate([np.where(r_in < STEP, (tiles - GROUP) / H, 0.0), np.where(r_in < STEP, GROUP / H, 0.0),
                            np.where(r_in < STEP, 0.0, 1 / H)], axis=1)
    share = np.repeat(share[:, :, None], 2, axis=2).astype(np.float32)
    of_group, of_channel = (c_in // 2 == (m // ROWS) // 2) / 2, c_in == m // ROWS
    sums_w = np.stack([of_group, of_channel - of_group, (c_in == c_out) & (r_in == 0)], axis=1).astype(np.float32)
    identity = ((c_in == c_out) & (r_in == r_out)).astype(np.float32)

    arrays = {
        "x_dram": x,
        "expert_rows_dram": expert_rows,
        "bias_dram": np.ascontiguousarray(L0_conv_bias).reshape(C, 1),
        "fc_wT_dram": np.ascontiguousarray(np.asarray(L0_conv_fc_w).T),
        "fc_b_dram": np.ascontiguousarray(L0_conv_fc_b).reshape(1, E),
        "share_dram": share,
        "sums_w_dram": sums_w,
        "identity_dram": identity,
    }
    nc = bacc.Bacc("TRN2", target_bir_lowering=False, num_devices=1, dynamic_dma_scratch_size=1024)
    args = [nc.dram_tensor(n, a.shape, mybir.dt.from_np(a.dtype), kind="ExternalInput").ap() for n, a in arrays.items()]
    args.append(nc.dram_tensor("out_dram", x.shape, mybir.dt.from_np(x.dtype), kind="ExternalOutput").ap())
    conv_kernel(nc, *args)
    return run_bass_kernel_spmd(nc, [arrays], core_ids=[0]).results[0]["out_dram"]
```

```python
from contextlib import ExitStack

import concourse.bass as bass
from concourse import mybir

F32 = mybir.dt.float32
F32R = mybir.dt.float32r
ALU = mybir.AluOpType
ACT = mybir.ActivationFunctionType
AX_X = mybir.AxisListType.X

P = 128
EPS = 1e-5
ROWS = 8
STEP = ROWS - 2
GROUP = 5
RING_GROUPS = 18
AHEAD = 2
STATS = 6
KW = 3


def conv_kernel(nc, x, expert_rows, bias, fc_wT, fc_b, share, sums_w, outputs_w, identity, out):
    B, C, H, W = x.shape
    E = fc_wT.shape[1]
    TILES = (H - 2) // STEP
    GROUPS = TILES // GROUP
    ALL_GROUPS = B * GROUPS
    INNER = STEP * C
    EARLY = TILES - GROUP
    assert C * ROWS == P and TILES * STEP + 2 == H and GROUPS * GROUP == TILES and GROUPS + 1 == RING_GROUPS
    assert 2 * KW * P <= W * 2 and 0 < AHEAD < GROUP

    with ExitStack() as ctx:
        def sb(name, shape, dt=F32):
            return ctx.enter_context(nc.sbuf_tensor(name, shape, dt))

        def sem(name):
            return ctx.enter_context(nc.semaphore(name))

        tiles = sb("tiles", [P, RING_GROUPS * GROUP * W])
        x_hi = sb("x_hi", [P, GROUP, W + 2], F32R)
        x_lo = sb("x_lo", [P, GROUP, W + 2], F32R)
        results = sb("results", [P, GROUP, W])
        bands = sb("bands", [P, E, KW, P])
        w_hi = sb("w_hi", [P, KW, P], F32R)
        w_lo = sb("w_lo", [P, KW, P], F32R)
        centre = sb("centre", [P, P])
        sums_sb = sb("sums_sb", [P, 3, P])
        ones = sb("ones", [P, P])
        stats = sb("stats", [P, TILES, STATS])
        share_sb = sb("share_sb", [P, 3, 2])
        fc_w_sb = sb("fc_w_sb", [P, E])
        fc_b_sb = sb("fc_b_sb", [P, E])
        bias_sb = sb("bias_sb", [P, 1])
        numbers = sb("numbers", [P, 72 + 2 * B])
        taken = [0]

        def few(count, parts=1):
            start = taken[0]
            taken[0] += count * parts
            assert taken[0] <= 72 + 2 * B
            view = numbers[:, start:taken[0]]
            return view if parts == 1 else view.rearrange("p (a b) -> p a b", b=parts)

        mean_var = few(3, 2)
        shared = few(3, 2)
        mean_sum = few(1)
        means = few(3)
        neg_mean = few(B)
        out_conv_bias = few(1)
        next_bias = few(1)
        out_bias = few(1)
        deviation = few(3)
        share_dev = few(3)
        var_terms = few(4)
        var_sum = few(1)
        var_eps = few(1)
        minus_half = few(1)
        rstd = few(1)
        fc_terms = few(E)
        fc_in = few(E)
        logit_max = few(1)
        logits = few(E)
        expd = few(E)
        exp_sum = few(1)
        inv_sum = few(1)
        mix = few(E)

        acc = ctx.enter_context(nc.psum_tensor("acc", [P, GROUP, W], F32))
        small = ctx.enter_context(nc.psum_tensor("small", [P, 3, W], F32))
        mean_sums, bias_sum, variance, logit_sum = small[:, 0, 0:3], small[:, 0, 3:4], small[:, 1, 0:1], small[:, 2, 0:E]
        w_full = small[:, 1, P:P + KW * P].rearrange("p (k m) -> p k m", k=KW)

        PARTS = ROWS + 2
        flat = results[:].rearrange("p i w -> p (i w)")
        row_flat = flat[:, 0:PARTS * E * KW * C]
        row_parts = row_flat.rearrange("p (j k c) -> p j k c", j=PARTS, c=C)
        to_outputs = flat[:, PARTS * E * KW * C:PARTS * E * KW * C + P]
        assert PARTS * E * KW * C + P <= GROUP * W

        x_loaded = [sem(f"x_loaded{i}") for i in range(GROUP)]
        y_stored = [sem(f"y_stored{i}") for i in range(GROUP)]
        top_stored = sem("top_stored")
        bottom_stored = sem("bottom_stored")
        const_loaded = sem("const_loaded")
        rows_loaded = sem("rows_loaded")
        zeroed = sem("zeroed")
        half_ready = sem("half_ready")
        setup_done = sem("setup_done")
        bias_summed = sem("bias_summed")
        dve_step = sem("dve_step")
        stats_done = sem("stats_done")
        aggregated = sem("aggregated")
        mean_summed = sem("mean_summed")
        means_ready = sem("means_ready")
        centred = sem("centred")
        var_summed = sem("var_summed")
        variance_ready = sem("variance_ready")
        var_eps_ready = sem("var_eps_ready")
        rstd_ready = sem("rstd_ready")
        fc_in_ready = sem("fc_in_ready")
        next_bias_ready = sem("next_bias_ready")
        out_bias_ready = sem("out_bias_ready")
        logits_summed = sem("logits_summed")
        logits_ready = sem("logits_ready")
        exp_ready = sem("exp_ready")
        weights_ready = sem("weights_ready")
        shift_done = sem("shift_done")
        hi_ready = sem("hi_ready")
        lo_ready = sem("lo_ready")
        ends_ready = sem("ends_ready")
        conv_done = sem("conv_done")
        y_ready = sem("y_ready")

        held_before = [0]

        def held(eng, name, value, most):
            held_before[0] += 1
            register = eng.alloc_register(f"{name}{held_before[0]}")
            eng.reg_mov(register, value)
            return eng.snap(register, donate=True, min_val=0, max_val=most)

        def ring_start(eng, g, name="ring_at"):
            return held(eng, name, (g % RING_GROUPS) * (GROUP * W), (RING_GROUPS - 1) * GROUP * W)

        def slot(start, i):
            return tiles[:, bass.ds(start + i * W, W)]

        def dram_rows(t, row, count):
            whole = bass.AP(tensor=t.tensor, offset=0, ap=[[H * W, C], [1, (B - 1) * C * H * W + H * W]])
            return whole[:, bass.ds(row * W, count * W)]

        block = ctx.enter_context(nc.Block())

        @block.sync
        def _(sp):
            def first_row(g, name):
                return held(sp, name, (g // GROUPS) * (C * H) + (g % GROUPS) * (GROUP * STEP),
                            (B - 1) * C * H + (GROUPS - 1) * GROUP * STEP)

            def load(at, src, i):
                sp.dma_start(slot(at, i), dram_rows(x, src + i * STEP, ROWS)).then_inc(x_loaded[i], 16)

            def store(g, dst, i):
                sp.wait_ge(y_ready, g * GROUP + i + 1)
                sp.dma_start(dram_rows(out, dst + i * STEP + 1, STEP), results[0:INNER, i]).then_inc(y_stored[i], 16)

            for i in range(GROUP):
                load(0, 0, i)
            with sp.Fori(1, RING_GROUPS) as g:
                at, src = ring_start(sp, g), first_row(g, "load_at")
                for i in range(GROUP):
                    sp.wait_ge(x_loaded[i], 16 * g)
                    load(at, src, i)

            def turn(g, stores=True):
                at, src = ring_start(sp, g), first_row(g + RING_GROUPS, "load_at")
                if stores:
                    dst = first_row(g - 1, "store_at")
                loaded = held(sp, "loaded_count", (g + RING_GROUPS) * 16, 16 * ALL_GROUPS)
                for i in range(GROUP):
                    sp.wait_ge(lo_ready, g * GROUP + i + 1)
                    sp.wait_ge(x_loaded[i], loaded)
                    load(at, src, i)
                    if stores:
                        store(g - 1, dst, i)

            turn(0, stores=False)
            with sp.Fori(1, ALL_GROUPS - RING_GROUPS) as g:
                turn(g)
            with sp.Fori(ALL_GROUPS - RING_GROUPS - 1, ALL_GROUPS) as g:
                dst = first_row(g, "store_at")
                for i in range(GROUP):
                    store(g, dst, i)
            for i in range(GROUP):
                sp.wait_ge(y_stored[i], 16 * ALL_GROUPS)
            sp.wait_ge(top_stored, 16 * B)
            sp.wait_ge(bottom_stored, 16 * B)

        @block.gpsimd
        def _(pool):
            pool.memset(minus_half[:], -0.5).then_inc(half_ready, 1)
            pool.dma_start(sums_sb[:], sums_w).then_inc(const_loaded, 16)
            pool.dma_start(to_outputs, outputs_w).then_inc(const_loaded, 16)
            pool.dma_start(centre[:], identity).then_inc(const_loaded, 16)
            pool.dma_start(share_sb[:], share).then_inc(const_loaded, 16)
            pool.wait_ge(zeroed, 4)
            pool.dma_start(fc_b_sb[0:1, :], fc_b).then_inc(const_loaded, 16)
            pool.dma_start(bias_sb[0:P:ROWS, :], bias).then_inc(const_loaded, 16)
            pool.dma_start(fc_w_sb[0:P:ROWS, :], fc_wT).then_inc(const_loaded, 16)
            for j in range(ROWS):
                for kh in range(3):
                    r = j + kh - 1
                    if 0 <= r < ROWS:
                        pool.dma_start(row_parts[r:P:ROWS, j], expert_rows[kh]).then_inc(rows_loaded, 16)
            pool.dma_start(row_parts[1:P:ROWS, ROWS], expert_rows[0]).then_inc(rows_loaded, 16)
            pool.dma_start(row_parts[ROWS - 2:P:ROWS, ROWS + 1], expert_rows[2]).then_inc(rows_loaded, 16)

            def inverse_deviation(s):
                pool.wait_ge(var_eps_ready, s + 1)
                nc.gpsimd.tensor_tensor(rstd[:], var_eps[:], minus_half[:], ALU.pow).then_inc(rstd_ready, 1)

            def store_edge(s, t, row, partition, stored):
                dst = held(pool, "store_at", s * (C * H), (B - 1) * C * H)
                pool.wait_ge(y_ready, s * TILES + t + 1)
                pool.dma_start(dram_rows(out, dst + row, 1), results[partition:partition + C, t % GROUP]
                               ).then_inc(stored, 16)

            pool.wait_ge(half_ready, 1)
            tile_count = pool.alloc_register("tile_count")
            pool.reg_mov(tile_count, 1)

            def ends(i):
                pool.wait_ge(lo_ready, tile_count)
                pool.reg_add(tile_count, tile_count, 1)
                for part in (x_lo[:, i], x_hi[:, i]):
                    nc.gpsimd.tensor_copy(part[:, 0:W + 2:W + 1], part[:, 2:W:W - 3]).then_inc(ends_ready, 1)

            def group_ends():
                for i in range(GROUP):
                    ends(i)

            def sample(s, first=False, last=False):
                group_ends()
                if not first:
                    store_edge(s - 1, TILES - 1, H - 1, INNER + C, bottom_stored)
                for i in range(GROUP):
                    ends(i)
                    if i == 0:
                        store_edge(s, 0, 0, INNER, top_stored)
                with pool.Fori(2, GROUPS):
                    group_ends()
                if not last:
                    inverse_deviation(s + 1)

            inverse_deviation(0)
            sample(0, first=True)
            with pool.Fori(1, B - 1) as s:
                sample(s)
            sample(B - 1, last=True)
            store_edge(B - 1, TILES - 1, H - 1, INNER + C, bottom_stored)

        @block.tensor
        def _(pe):
            def sum_means(s):
                pe.wait_ge(mean_summed, s + 1)
                for what in range(3):
                    mm = pe.matmul(mean_sums[:, what:what + 1], sums_sb[:, what, :], mean_sum[:], start=True, stop=True)
                mm.then_inc(means_ready, 1)

            def sum_variance(s):
                pe.wait_ge(var_summed, s + 1)
                pe.matmul(variance, sums_sb[:, 0, :], var_sum[:], start=True, stop=True).then_inc(variance_ready, 1)

            def sum_logits(s):
                pe.wait_ge(fc_in_ready, s + 1)
                pe.matmul(logit_sum, ones[:, :], fc_in[:, :], start=True, stop=True).then_inc(logits_summed, 1)

            def conv(s, j, i, fresh_banks=False, fresh_weights=False, last_of_sample=False):
                n = (s * GROUPS + j) * GROUP + i
                pe.wait_ge(ends_ready, 2 * (n + 1))
                if not fresh_banks:
                    pe.wait_ge(y_ready, n - GROUP + 1)
                for k in range(KW):
                    if fresh_weights:
                        pe.wait_ge(weights_ready, s * KW + k + 1)
                    for w, part in ((w_hi, x_hi), (w_lo, x_hi), (w_hi, x_lo)):
                        mm = pe.matmul(acc[:, i, :], w[:, k, :], part[:, i, k:k + W],
                                       start=k == 0 and w is w_hi and part is x_hi,
                                       stop=k == KW - 1 and part is x_lo)
                    if last_of_sample and k < KW - 1:
                        mm.then_inc(shift_done, 1)
                mm.then_inc(conv_done, 1)

            def sample(s, first=False, last=False):
                for i in range(GROUP):
                    conv(s, 0, i, fresh_banks=first, fresh_weights=i == 0)
                with pe.Fori(1, GROUPS - 1) as j:
                    for i in range(GROUP):
                        conv(s, j, i)
                for i in range(GROUP):
                    if not last and i < 3:
                        (sum_means, sum_variance, sum_logits)[i](s + 1)
                    conv(s, GROUPS - 1, i, last_of_sample=i == GROUP - 1)

            pe.wait_ge(const_loaded, 16 * 7)
            pe.matmul(bias_sum, to_outputs, bias_sb[:], start=True, stop=True).then_inc(bias_summed, 1)
            pe.wait_ge(setup_done, 1)
            sum_means(0)
            sum_variance(0)
            sum_logits(0)
            sample(0, first=True)
            with pe.Fori(1, B - 1) as s:
                sample(s)
            sample(B - 1, last=True)

        @block.scalar
        def _(act):
            def high(s, at, i):
                act.activation(x_hi[:, i, 1:W + 1], slot(at, i), ACT.Identity,
                               bias=neg_mean[:, bass.ds(s, 1)]).then_inc(hi_ready, 1)

            def result(s, j, i, first=False):
                g = s * GROUPS + j
                if not first:
                    act.wait_ge(y_stored[i], 16 * g)
                act.wait_ge(conv_done, g * GROUP + i + 1)
                act.activation(results[:, i], acc[:, i, :], ACT.Identity,
                               bias=out_bias[:, 0:1]).then_inc(y_ready, 1)

            def exponentials(s):
                act.wait_ge(logits_ready, s + 1)
                act.activation(expd[:], logits[:], ACT.Exp, accum_out=exp_sum[:]).then_inc(exp_ready, 1)

            def inside(s, first=False):
                at = ring_start(act, s * GROUPS + 1)
                for i in range(GROUP):
                    if i == GROUP - 1 and not first:
                        act.wait_ge(bottom_stored, 16 * s)
                    result(s, 0, i, first)
                    high(s, at, i)
                act.wait_ge(top_stored, 16 * (s + 1))
                with act.Fori(2, GROUPS) as j:
                    at = ring_start(act, s * GROUPS + j)
                    for i in range(GROUP):
                        result(s, j - 1, i)
                        high(s, at, i)

            def sample(s, first=False):
                inside(s, first)
                at = ring_start(act, (s + 1) * GROUPS)
                for i in range(GROUP):
                    result(s, GROUPS - 1, i)
                    if i == 0:
                        act.wait_ge(centred, s + 2)
                    high(s + 1, at, i)
                    if i == 1:
                        exponentials(s + 1)
                act.wait_ge(next_bias_ready, s + 2)
                act.wait_ge(y_ready, (s + 1) * TILES)
                act.activation(out_bias[:], next_bias[:], ACT.Identity).then_inc(out_bias_ready, 1)
                act.wait_ge(out_bias_ready, s + 2)

            act.wait_ge(centred, 1)
            for i in range(GROUP):
                high(0, 0, i)
            exponentials(0)
            act.wait_ge(next_bias_ready, 1)
            act.activation(out_bias[:], next_bias[:], ACT.Identity).then_inc(out_bias_ready, 1)
            act.wait_ge(out_bias_ready, 1)
            sample(0, first=True)
            with act.Fori(1, B - 1) as s:
                sample(s)
            inside(B - 1)
            for i in range(GROUP):
                result(B - 1, GROUPS - 1, i)

        @block.vector
        def _(dve):
            SETUP = 1 + ROWS + 1
            STEPS = 15
            done = [0]

            def link(ins, base=0):
                done[0] += 1
                ins.then_inc(dve_step, 1)
                dve.wait_ge(dve_step, base + done[0])

            def low(s, n, at, i):
                dve.wait_ge(hi_ready, n + 1)
                dve.scalar_tensor_tensor(x_lo[:, i, 1:W + 1], slot(at, i), neg_mean[:, bass.ds(s, 1)],
                                         x_hi[:, i, 1:W + 1].bitcast(F32), ALU.add, ALU.subtract
                                         ).then_inc(lo_ready, 1)

            def tile_stats(g, j, at, i):
                dve.wait_ge(x_loaded[i], 16 * (g + 1))
                dve.bn_stats(stats[:, bass.ds(j * GROUP + i, 1), :].rearrange("p o k -> p (o k)"),
                             slot(at, i)).then_inc(stats_done, 1)

            def group_mean_and_variance(s):
                base = STEPS * s + SETUP
                done[0] = 0
                dve.wait_ge(stats_done, TILES * (s + 1))
                dve.memset(var_terms[:], 0.0)
                dve.bn_aggr(mean_var[:, 0, :], stats[:, 0:EARLY, :]).then_inc(aggregated, 1)
                dve.bn_aggr(mean_var[:, 1, :], stats[:, EARLY:TILES, :]).then_inc(aggregated, 1)
                dve.bn_aggr(mean_var[:, 2, :], stats[:, TILES - 1, :]).then_inc(aggregated, 1)
                dve.wait_ge(aggregated, 3 * (s + 1))
                link(dve.tensor_tensor(shared[:], mean_var[:], share_sb[:], ALU.mult), base)
                dve.reduce_sum(mean_sum[:], shared[:, :, 0], AX_X).then_inc(mean_summed, 1)
                link(dve.reduce_sum(var_terms[:, 3:4], shared[:, :, 1], AX_X), base)

            def centre_and_spread(s):
                base = STEPS * s + SETUP
                dve.wait_ge(means_ready, s + 1)
                link(dve.tensor_copy(means[:], mean_sums), base)
                dve.tensor_scalar(neg_mean[:, bass.ds(s, 1)], means[:, 0:1], -1.0, None, ALU.mult).then_inc(centred, 1)
                dve.tensor_scalar(deviation[:], mean_var[:, :, 0], means[:, 0:1], None, ALU.subtract)
                link(dve.scalar_tensor_tensor(share_dev[:], mean_var[:, :, 0], means[:, 0:1], share_sb[:, :, 0],
                                              ALU.subtract, ALU.mult), base)
                link(dve.tensor_tensor(var_terms[:, 0:3], deviation[:], share_dev[:], ALU.mult), base)
                dve.reduce_sum(var_sum[:], var_terms[:], AX_X).then_inc(var_summed, 1)
                dve.tensor_tensor(next_bias[:], out_conv_bias[:], means[:, 2:3], ALU.add).then_inc(next_bias_ready, 1)
                link(dve.tensor_scalar(fc_terms[:], fc_w_sb[:], means[:, 1:2], None, ALU.mult), base)

            def scale(s):
                dve.wait_ge(variance_ready, s + 1)
                dve.tensor_scalar(var_eps[:], variance, EPS, None, ALU.add).then_inc(var_eps_ready, 1)
                dve.wait_ge(rstd_ready, s + 1)
                dve.scalar_tensor_tensor(fc_in[:], fc_terms[:], rstd[:, 0:1], fc_b_sb[:],
                                         ALU.mult, ALU.add).then_inc(fc_in_ready, 1)

            def softmax_input(s):
                base = STEPS * s + SETUP
                dve.wait_ge(logits_summed, s + 1)
                link(dve.reduce_max(logit_max[:], logit_sum, AX_X), base)
                dve.tensor_scalar(logits[:], logit_sum, logit_max[:, 0:1], None, ALU.subtract).then_inc(logits_ready, 1)

            def mixed_weights(s):
                base = STEPS * s + SETUP
                dve.wait_ge(exp_ready, s + 1)
                link(dve.reciprocal(inv_sum[:], exp_sum[:]), base)
                link(dve.tensor_scalar(mix[:], expd[:], inv_sum[:, 0:1], rstd[:, 0:1], ALU.mult, ALU.mult), base)
                dve.tensor_scalar(w_full[:, 0:KW:2], bands[:, 0, 0:KW:2], mix[:, 0:1], None, ALU.mult)
                link(dve.scalar_tensor_tensor(w_full[:, 1], bands[:, 0, 1], mix[:, 0:1], centre[:],
                                              ALU.mult, ALU.add), base)
                for e in range(1, E):
                    link(dve.scalar_tensor_tensor(w_full[:], bands[:, e], mix[:, e:e + 1], w_full[:],
                                                  ALU.mult, ALU.add), base)

            def weight_parts(s):
                base = STEPS * s + SETUP
                for k in range(KW):
                    if not isinstance(s, int) or s > 0:
                        if k < KW - 1:
                            dve.wait_ge(shift_done, (s - 1) * (KW - 1) + k + 1)
                        else:
                            dve.wait_ge(conv_done, s * TILES)
                    link(dve.tensor_copy(w_hi[:, k], w_full[:, k]), base)
                    dve.tensor_tensor(w_lo[:, k], w_full[:, k], w_hi[:, k].bitcast(F32),
                                      ALU.subtract).then_inc(weights_ready, 1)
                assert done[0] == STEPS, done

            def stats_ahead(g, j, i, at, at_after):
                if i + AHEAD < GROUP:
                    tile_stats(g + GROUPS, j, at, i + AHEAD)
                else:
                    tile_stats(g + GROUPS + 1, j + 1, at_after, i + AHEAD - GROUP)

            def inner_turns(s, ahead):
                with dve.Fori(1, GROUPS - 1) as j:
                    g = s * GROUPS + j
                    at = ring_start(dve, g)
                    if ahead:
                        at_next = ring_start(dve, g + GROUPS, "ring_next")
                        at_after = ring_start(dve, g + GROUPS + 1, "ring_after")
                    for i in range(GROUP):
                        low(s, g * GROUP + i, at, i)
                        if ahead:
                            stats_ahead(g, j, i, at_next, at_after)

            def boundary(s, ahead=True):
                g = s * GROUPS + GROUPS - 1
                at = ring_start(dve, g)
                at_next = ring_start(dve, g + GROUPS, "ring_next")
                at_first = ring_start(dve, g + 1, "ring_first")
                if ahead:
                    at_after = ring_start(dve, g + GROUPS + 1, "ring_after")
                    at_second = ring_start(dve, g + GROUPS + 2, "ring_second")

                def first_low(i):
                    low(s + 1, (g + 1) * GROUP + i, at_first, i)

                for i in range(GROUP):
                    if i == GROUP - 1:
                        centre_and_spread(s + 1)
                    low(s, g * GROUP + i, at, i)
                    if i + AHEAD < GROUP:
                        tile_stats(g + GROUPS, GROUPS - 1, at_next, i + AHEAD)
                    elif ahead:
                        tile_stats(g + GROUPS + 1, 0, at_after, i + AHEAD - GROUP)
                    if i + AHEAD == GROUP - 1:
                        group_mean_and_variance(s + 1)
                scale(s + 1)
                first_low(0)
                softmax_input(s + 1)
                if ahead:
                    stats_ahead(g + 1, 0, 0, at_after, at_second)
                first_low(1)
                mixed_weights(s + 1)
                first_low(2)
                weight_parts(s + 1)
                for i in range(1, GROUP):
                    if i > 2:
                        first_low(i)
                    if ahead:
                        stats_ahead(g + 1, 0, i, at_after, at_second)

            dve.memset(row_flat, 0.0).then_inc(zeroed, 1)
            dve.memset(bias_sb[:], 0.0).then_inc(zeroed, 1)
            dve.memset(fc_w_sb[:], 0.0).then_inc(zeroed, 1)
            dve.memset(fc_b_sb[:], 0.0).then_inc(zeroed, 1)
            link(dve.memset(ones[:], 1.0))
            dve.wait_ge(const_loaded, 16 * 7)
            dve.wait_ge(rows_loaded, 16 * 3 * ROWS)
            cols = bands[:].rearrange("p e k m -> p (e k) m")
            edge = {0: INNER, ROWS - 1: INNER + C}
            for j in range(ROWS):
                if j in edge:
                    link(dve.tensor_tensor(cols[:, :, edge[j]:edge[j] + C], row_parts[:, j],
                                           row_parts[:, ROWS + (j > 0)], ALU.add))
                else:
                    link(dve.tensor_copy(cols[:, :, j - 1:INNER:STEP], row_parts[:, j]))
            dve.wait_ge(bias_summed, 1)
            link(dve.tensor_copy(out_conv_bias[:], bias_sum))
            assert done[0] == SETUP
            dve.memset(mix[:], 0.0).then_inc(setup_done, 1)
            with dve.Fori(0, GROUPS) as g:
                at = ring_start(dve, g)
                for i in range(GROUP):
                    tile_stats(g, g, at, i)
            group_mean_and_variance(0)
            centre_and_spread(0)
            scale(0)
            softmax_input(0)
            mixed_weights(0)
            low(0, 0, 0, 0)
            weight_parts(0)
            for i in range(1, GROUP):
                low(0, i, 0, i)
            for i in range(AHEAD + GROUP):
                g = GROUPS + i // GROUP
                tile_stats(g, i // GROUP, (g % RING_GROUPS) * GROUP * W, i % GROUP)
            with dve.Fori(0, B - 2) as s:
                inner_turns(s, True)
                boundary(s)
            inner_turns(B - 2, True)
            boundary(B - 2, ahead=False)
            inner_turns(B - 1, False)
            last = ALL_GROUPS - 1
            for i in range(GROUP):
                low(B - 1, last * GROUP + i, (last % RING_GROUPS) * GROUP * W, i)


def kernel(x, L0_conv_w_experts, L0_conv_bias, L0_conv_fc_w, L0_conv_fc_b):
    import numpy as np
    import concourse.bacc as bacc
    from concourse.bass_utils import run_bass_kernel_spmd

    x = np.ascontiguousarray(x)
    B, C, H, W = x.shape
    E = L0_conv_w_experts.shape[0]
    expert_rows = np.ascontiguousarray(
        np.asarray(L0_conv_w_experts).transpose(3, 2, 0, 4, 1)).reshape(3, C, E * 3, C)

    inner = STEP * C
    c_in, r_in = np.arange(P)[:, None] // ROWS, np.arange(P)[:, None] % ROWS
    m = np.arange(P)[None, :]
    c_out = np.where(m < inner, m // STEP, (m - inner) % C)
    r_out = np.where(m < inner, m % STEP + 1, np.where(m < inner + C, 0, ROWS - 1))
    tiles = (H - 2) // STEP
    share = np.concatenate([np.where(r_in < STEP, (tiles - GROUP) / H, 0.0), np.where(r_in < STEP, GROUP / H, 0.0),
                            np.where(r_in < STEP, 0.0, 1 / H)], axis=1)
    share = np.repeat(share[:, :, None], 2, axis=2).astype(np.float32)
    of_group, of_channel, of_out_group = (c_in // 2 == m // ROWS // 2) / 2, c_in == m // ROWS, (c_in // 2 == c_out // 2) / 2
    sums_w = np.stack([of_group, of_channel - of_group, of_out_group], axis=1).astype(np.float32)
    outputs_w = (c_in == c_out).astype(np.float32)
    identity = ((c_in == c_out) & (r_in == r_out)).astype(np.float32)

    arrays = {
        "x_dram": x,
        "expert_rows_dram": expert_rows,
        "bias_dram": np.ascontiguousarray(L0_conv_bias).reshape(C, 1),
        "fc_wT_dram": np.ascontiguousarray(np.asarray(L0_conv_fc_w).T),
        "fc_b_dram": np.ascontiguousarray(L0_conv_fc_b).reshape(1, E),
        "share_dram": share,
        "sums_w_dram": sums_w,
        "outputs_w_dram": outputs_w,
        "identity_dram": identity,
    }
    nc = bacc.Bacc("TRN2", target_bir_lowering=False, num_devices=1, dynamic_dma_scratch_size=256)
    args = [nc.dram_tensor(n, a.shape, mybir.dt.from_np(a.dtype), kind="ExternalInput").ap() for n, a in arrays.items()]
    args.append(nc.dram_tensor("out_dram", x.shape, mybir.dt.from_np(x.dtype), kind="ExternalOutput").ap())
    conv_kernel(nc, *args)
    return run_bass_kernel_spmd(nc, [arrays], core_ids=[0]).results[0]["out_dram"]
```

```python
from contextlib import ExitStack

import concourse.bass as bass
from concourse import mybir

F32 = mybir.dt.float32
F32R = mybir.dt.float32r
ALU = mybir.AluOpType
ACT = mybir.ActivationFunctionType
AX_X = mybir.AxisListType.X

P = 128
EPS = 1e-5
ROWS = 8
STEP = ROWS - 2
GROUP = 5
RING_GROUPS = 18
AHEAD = 2
STATS = 6
KW = 3


def conv_kernel(nc, x, expert_rows, bias, fc_wT, fc_b, constants, selections, out):
    B, C, H, W = x.shape
    E = fc_wT.shape[1]
    TILES = (H - 2) // STEP
    GROUPS = TILES // GROUP
    ALL_GROUPS = B * GROUPS
    INNER = STEP * C
    EARLY = TILES - GROUP
    assert C * ROWS == P and TILES * STEP + 2 == H and GROUPS * GROUP == TILES and GROUPS + 1 == RING_GROUPS
    assert 0 < AHEAD < GROUP

    with ExitStack() as ctx:
        def sb(name, shape, dt=F32):
            return ctx.enter_context(nc.sbuf_tensor(name, shape, dt))

        def sem(name):
            return ctx.enter_context(nc.semaphore(name))

        tiles = sb("tiles", [P, RING_GROUPS * GROUP * W])
        x_hi = sb("x_hi", [P, GROUP, W + 2], F32R)
        x_lo = sb("x_lo", [P, GROUP, W + 2], F32R)
        results = sb("results", [P, GROUP, W])
        bands = sb("bands", [P, E, KW, P])
        w_hi = sb("w_hi", [P, KW, P], F32R)
        w_lo = sb("w_lo", [P, KW, P], F32R)
        consts = sb("consts", [P, 3 * P + 3 * 2])
        group_w, out_group_w, centre = consts[:, 0:P], consts[:, P:2 * P], consts[:, 2 * P:3 * P]
        share_sb = consts[:, 3 * P:].rearrange("p (a b) -> p a b", b=2)
        ones = sb("ones", [P, P])
        stats = sb("stats", [P, TILES, STATS])
        fc_w_sb = sb("fc_w_sb", [P, E])
        fc_b_sb = sb("fc_b_sb", [P, E])
        numbers = sb("numbers", [P, 72 + 2 * B])
        taken = [0]

        def few(count, parts=1):
            start = taken[0]
            taken[0] += count * parts
            assert taken[0] <= 72 + 2 * B
            view = numbers[:, start:taken[0]]
            return view if parts == 1 else view.rearrange("p (a b) -> p a b", b=parts)

        mean_var = few(3, 2)
        shared = few(3, 2)
        mean_sum = few(1)
        means = few(2)
        channel_off = few(1)
        neg_mean = few(B)
        out_conv_bias = few(1)
        next_bias = few(1)
        out_bias = few(1)
        deviation = few(3)
        share_dev = few(3)
        var_terms = few(4)
        var_sum = few(1)
        var_eps = few(1)
        minus_half = few(1)
        rstd = few(1)
        fc_terms = few(E)
        fc_in = few(E)
        logit_max = few(1)
        logits = few(E)
        expd = few(E)
        exp_sum = few(1)
        inv_sum = few(1)
        mix = few(E)

        acc = ctx.enter_context(nc.psum_tensor("acc", [P, GROUP, W], F32))
        small = ctx.enter_context(nc.psum_tensor("small", [P, 3, W], F32))
        mean_sums, bias_sum = small[:, 0, 0:2], small[:, 0, 2:3]
        variance, logit_sum = small[:, 1, 0:1], small[:, 2, 0:E]
        assert P + KW * P <= W
        w_full = small[:, 1, P:P + KW * P].rearrange("p (k m) -> p k m", k=KW)

        TAPS, COLS = 3 * C, E * KW * C
        flat = results[0:TAPS].rearrange("p i w -> p (i w)")
        select = flat[:, 0:(ROWS + 1) * P].rearrange("p (j m) -> p j m", m=P)
        taps = flat[:, (ROWS + 1) * P:(ROWS + 1) * P + COLS]
        bias_sb = flat[0:C, (ROWS + 1) * P + COLS:(ROWS + 1) * P + COLS + 1]
        PER_BANK = W // COLS

        def band_columns(j):
            return acc[:, j // PER_BANK, (j % PER_BANK) * COLS:(j % PER_BANK + 1) * COLS]

        x_loaded = [sem(f"x_loaded{i}") for i in range(GROUP)]
        y_stored = [sem(f"y_stored{i}") for i in range(GROUP)]
        top_stored = sem("top_stored")
        bottom_stored = sem("bottom_stored")
        taps_loaded = sem("taps_loaded")
        const_loaded = sem("const_loaded")
        zeroed = sem("zeroed")
        half_ready = sem("half_ready")
        setup_done = sem("setup_done")
        bands_ready = sem("bands_ready")
        dve_step = sem("dve_step")
        stats_done = sem("stats_done")
        aggregated = sem("aggregated")
        mean_summed = sem("mean_summed")
        means_ready = sem("means_ready")
        centred = sem("centred")
        var_summed = sem("var_summed")
        variance_ready = sem("variance_ready")
        var_eps_ready = sem("var_eps_ready")
        rstd_ready = sem("rstd_ready")
        fc_in_ready = sem("fc_in_ready")
        next_bias_ready = sem("next_bias_ready")
        out_bias_ready = sem("out_bias_ready")
        logits_summed = sem("logits_summed")
        logits_ready = sem("logits_ready")
        exp_ready = sem("exp_ready")
        weights_ready = sem("weights_ready")
        shift_done = sem("shift_done")
        hi_ready = sem("hi_ready")
        lo_ready = sem("lo_ready")
        ends_ready = sem("ends_ready")
        conv_done = sem("conv_done")
        y_ready = sem("y_ready")

        held_before = [0]

        def held(eng, name, value, most):
            held_before[0] += 1
            register = eng.alloc_register(f"{name}{held_before[0]}")
            eng.reg_mov(register, value)
            return eng.snap(register, donate=True, min_val=0, max_val=most)

        def ring_start(eng, g, name="ring_at"):
            return held(eng, name, (g % RING_GROUPS) * (GROUP * W), (RING_GROUPS - 1) * GROUP * W)

        def slot(start, i):
            return tiles[:, bass.ds(start + i * W, W)]

        def dram_rows(t, row, count):
            whole = bass.AP(tensor=t.tensor, offset=0, ap=[[H * W, C], [1, (B - 1) * C * H * W + H * W]])
            return whole[:, bass.ds(row * W, count * W)]

        def first_row(eng, g, name):
            return held(eng, name, (g // GROUPS) * (C * H) + (g % GROUPS) * (GROUP * STEP),
                        (B - 1) * C * H + (GROUPS - 1) * GROUP * STEP)

        def load(eng, at, src, i):
            eng.dma_start(slot(at, i), dram_rows(x, src + i * STEP, ROWS)).then_inc(x_loaded[i], 16)

        def first_loads(eng, places):
            for i in places:
                load(eng, 0, 0, i)
            with eng.Fori(1, GROUPS) as g:
                at, src = ring_start(eng, g), first_row(eng, g, "load_at")
                for i in places:
                    eng.wait_ge(x_loaded[i], 16 * g)
                    load(eng, at, src, i)

        block = ctx.enter_context(nc.Block())

        @block.sync
        def _(sp):
            def store(g, dst, i):
                sp.wait_ge(y_ready, g * GROUP + i + 1)
                sp.dma_start(dram_rows(out, dst + i * STEP + 1, STEP), results[0:INNER, i]).then_inc(y_stored[i], 16)

            first_loads(sp, range(0, GROUP, 2))
            for i in range(GROUP):
                sp.wait_ge(x_loaded[i], 16 * GROUPS)
                load(sp, GROUPS * GROUP * W, C * H, i)

            def turn(g, stores=True):
                at, src = ring_start(sp, g), first_row(sp, g + RING_GROUPS, "load_at")
                if stores:
                    dst = first_row(sp, g - 1, "store_at")
                loaded = held(sp, "loaded_count", (g + RING_GROUPS) * 16, 16 * ALL_GROUPS)
                for i in range(GROUP):
                    sp.wait_ge(lo_ready, g * GROUP + i + 1)
                    sp.wait_ge(x_loaded[i], loaded)
                    load(sp, at, src, i)
                    if stores:
                        store(g - 1, dst, i)

            turn(0, stores=False)
            with sp.Fori(1, ALL_GROUPS - RING_GROUPS) as g:
                turn(g)
            with sp.Fori(ALL_GROUPS - RING_GROUPS - 1, ALL_GROUPS) as g:
                dst = first_row(sp, g, "store_at")
                for i in range(GROUP):
                    store(g, dst, i)
            for i in range(GROUP):
                sp.wait_ge(y_stored[i], 16 * ALL_GROUPS)
            sp.wait_ge(top_stored, 16 * B)
            sp.wait_ge(bottom_stored, 16 * B)

        @block.gpsimd
        def _(pool):
            pool.dma_start(flat[:, 0:(ROWS + 1) * P], selections).then_inc(taps_loaded, 16)
            pool.dma_start(taps, expert_rows).then_inc(taps_loaded, 16)
            pool.dma_start(bias_sb, bias).then_inc(taps_loaded, 16)
            pool.dma_start(consts[:], constants).then_inc(const_loaded, 16)
            pool.dma_start(fc_w_sb[:], bass.AP(tensor=fc_wT.tensor, offset=0, ap=[[E, C], [0, ROWS], [1, E]])
                           ).then_inc(const_loaded, 16)
            pool.wait_ge(zeroed, 1)
            pool.dma_start(fc_b_sb[0:1, :], fc_b).then_inc(const_loaded, 16)
            pool.memset(minus_half[:], -0.5).then_inc(half_ready, 1)

            def inverse_deviation(s):
                pool.wait_ge(var_eps_ready, s + 1)
                nc.gpsimd.tensor_tensor(rstd[:], var_eps[:], minus_half[:], ALU.pow).then_inc(rstd_ready, 1)

            def store_edge(s, t, row, partition, stored):
                dst = held(pool, "store_at", s * (C * H), (B - 1) * C * H)
                pool.wait_ge(y_ready, s * TILES + t + 1)
                pool.dma_start(dram_rows(out, dst + row, 1), results[partition:partition + C, t % GROUP]
                               ).then_inc(stored, 16)

            pool.wait_ge(half_ready, 1)
            tile_count = pool.alloc_register("tile_count")
            pool.reg_mov(tile_count, 1)

            def ends(i):
                pool.wait_ge(lo_ready, tile_count)
                pool.reg_add(tile_count, tile_count, 1)
                for part in (x_lo[:, i], x_hi[:, i]):
                    nc.gpsimd.tensor_copy(part[:, 0:W + 2:W + 1], part[:, 2:W:W - 3]).then_inc(ends_ready, 1)

            def group_ends():
                for i in range(GROUP):
                    ends(i)

            def sample(s, first=False, last=False):
                group_ends()
                if not first:
                    store_edge(s - 1, TILES - 1, H - 1, INNER + C, bottom_stored)
                for i in range(GROUP):
                    ends(i)
                    if i == 0:
                        store_edge(s, 0, 0, INNER, top_stored)
                with pool.Fori(2, GROUPS):
                    group_ends()
                if not last:
                    inverse_deviation(s + 1)

            inverse_deviation(0)
            sample(0, first=True)
            with pool.Fori(1, B - 1) as s:
                sample(s)
            sample(B - 1, last=True)
            store_edge(B - 1, TILES - 1, H - 1, INNER + C, bottom_stored)

        @block.tensor
        def _(pe):
            def sum_means(s):
                pe.wait_ge(mean_summed, s + 1)
                pe.matmul(mean_sums[:, 0:1], group_w, mean_sum[:], start=True, stop=True)
                pe.matmul(mean_sums[:, 1:2], out_group_w, mean_sum[:], start=True, stop=True).then_inc(means_ready, 1)

            def sum_variance(s):
                pe.wait_ge(var_summed, s + 1)
                pe.matmul(variance, group_w, var_sum[:], start=True, stop=True).then_inc(variance_ready, 1)

            def sum_logits(s):
                pe.wait_ge(fc_in_ready, s + 1)
                pe.matmul(logit_sum, ones[:, :], fc_in[:, :], start=True, stop=True).then_inc(logits_summed, 1)

            def conv(s, j, i, fresh_banks=False, fresh_weights=False, last_of_sample=False):
                n = (s * GROUPS + j) * GROUP + i
                pe.wait_ge(ends_ready, 2 * (n + 1))
                if not fresh_banks:
                    pe.wait_ge(y_ready, n - GROUP + 1)
                for k in range(KW):
                    if fresh_weights:
                        pe.wait_ge(weights_ready, s * KW + k + 1)
                    for w, part in ((w_hi, x_hi), (w_hi, x_lo), (w_lo, x_hi)):
                        mm = pe.matmul(acc[:, i, :], w[:, k, :], part[:, i, k:k + W],
                                       start=k == 0 and w is w_hi and part is x_hi,
                                       stop=k == KW - 1 and w is w_lo)
                    if last_of_sample and k < KW - 1:
                        mm.then_inc(shift_done, 1)
                mm.then_inc(conv_done, 1)

            def sample(s, first=False, last=False):
                for i in range(GROUP):
                    conv(s, 0, i, fresh_banks=first, fresh_weights=i == 0)
                with pe.Fori(1, GROUPS - 1) as j:
                    for i in range(GROUP):
                        conv(s, j, i)
                for i in range(GROUP):
                    if not last and i < 3:
                        (sum_means, sum_variance, sum_logits)[i](s + 1)
                    conv(s, GROUPS - 1, i, last_of_sample=i == GROUP - 1)

            pe.wait_ge(taps_loaded, 16 * 3)
            for j in range(ROWS):
                pe.matmul(band_columns(j), select[:, j], taps, start=True, stop=True)
            pe.matmul(bias_sum, select[0:C, ROWS], bias_sb, start=True, stop=True).then_inc(bands_ready, 1)
            pe.wait_ge(setup_done, 1)
            sum_means(0)
            sum_variance(0)
            sum_logits(0)
            sample(0, first=True)
            with pe.Fori(1, B - 1) as s:
                sample(s)
            sample(B - 1, last=True)

        @block.scalar
        def _(act):
            def high(s, at, i):
                act.activation(x_hi[:, i, 1:W + 1], slot(at, i), ACT.Identity,
                               bias=neg_mean[:, bass.ds(s, 1)]).then_inc(hi_ready, 1)

            def result(s, j, i, first=False):
                g = s * GROUPS + j
                if not first:
                    act.wait_ge(y_stored[i], 16 * g)
                act.wait_ge(conv_done, g * GROUP + i + 1)
                act.activation(results[:, i], acc[:, i, :], ACT.Identity,
                               bias=out_bias[:, 0:1]).then_inc(y_ready, 1)

            def exponentials(s):
                act.wait_ge(logits_ready, s + 1)
                act.activation(expd[:], logits[:], ACT.Exp, accum_out=exp_sum[:]).then_inc(exp_ready, 1)

            def inside(s, first=False):
                at = ring_start(act, s * GROUPS + 1)
                for i in range(GROUP):
                    if i == GROUP - 1 and not first:
                        act.wait_ge(bottom_stored, 16 * s)
                    result(s, 0, i, first)
                    high(s, at, i)
                act.wait_ge(top_stored, 16 * (s + 1))
                with act.Fori(2, GROUPS) as j:
                    at = ring_start(act, s * GROUPS + j)
                    for i in range(GROUP):
                        result(s, j - 1, i)
                        high(s, at, i)

            def sample(s, first=False):
                inside(s, first)
                at = ring_start(act, (s + 1) * GROUPS)
                for i in range(GROUP):
                    result(s, GROUPS - 1, i)
                    if i == 0:
                        act.wait_ge(centred, s + 2)
                    high(s + 1, at, i)
                    if i == 1:
                        exponentials(s + 1)
                act.wait_ge(next_bias_ready, s + 2)
                act.wait_ge(y_ready, (s + 1) * TILES)
                act.activation(out_bias[:], next_bias[:], ACT.Identity).then_inc(out_bias_ready, 1)
                act.wait_ge(out_bias_ready, s + 2)

            first_loads(act, range(1, GROUP, 2))
            act.wait_ge(centred, 1)
            for i in range(GROUP):
                high(0, 0, i)
            exponentials(0)
            act.wait_ge(next_bias_ready, 1)
            act.activation(out_bias[:], next_bias[:], ACT.Identity).then_inc(out_bias_ready, 1)
            act.wait_ge(out_bias_ready, 1)
            sample(0, first=True)
            with act.Fori(1, B - 1) as s:
                sample(s)
            inside(B - 1)
            for i in range(GROUP):
                result(B - 1, GROUPS - 1, i)

        @block.vector
        def _(dve):
            SETUP = 2
            STEPS = 16
            done = [0]

            def link(ins, base=0):
                done[0] += 1
                ins.then_inc(dve_step, 1)
                dve.wait_ge(dve_step, base + done[0])

            def low(s, n, at, i):
                dve.wait_ge(hi_ready, n + 1)
                dve.scalar_tensor_tensor(x_lo[:, i, 1:W + 1], slot(at, i), neg_mean[:, bass.ds(s, 1)],
                                         x_hi[:, i, 1:W + 1].bitcast(F32), ALU.add, ALU.subtract
                                         ).then_inc(lo_ready, 1)

            def tile_stats(g, j, at, i):
                dve.wait_ge(x_loaded[i], 16 * (g + 1))
                dve.bn_stats(stats[:, bass.ds(j * GROUP + i, 1), :].rearrange("p o k -> p (o k)"),
                             slot(at, i)).then_inc(stats_done, 1)

            def early_statistics(s):
                dve.wait_ge(stats_done, TILES * s + EARLY)
                dve.memset(var_terms[:], 0.0)
                dve.bn_aggr(mean_var[:, 0, :], stats[:, 0:EARLY, :]).then_inc(aggregated, 1)

            def statistics(s):
                base = STEPS * s + SETUP
                done[0] = 0
                dve.wait_ge(stats_done, TILES * (s + 1))
                dve.memset(deviation[:], 0.0)
                dve.bn_aggr(mean_var[:, 1, :], stats[:, EARLY:TILES, :]).then_inc(aggregated, 1)
                dve.bn_aggr(mean_var[:, 2, :], stats[:, TILES - 1, :]).then_inc(aggregated, 1)
                dve.wait_ge(aggregated, 3 * (s + 1))
                link(dve.tensor_tensor(shared[:], mean_var[:], share_sb, ALU.mult), base)
                dve.reduce_sum(mean_sum[:], shared[:, :, 0], AX_X).then_inc(mean_summed, 1)
                link(dve.reduce_sum(var_terms[:, 3:4], shared[:, :, 1], AX_X), base)

            def centre_and_spread(s):
                base = STEPS * s + SETUP
                dve.wait_ge(means_ready, s + 1)
                link(dve.tensor_copy(means[:], mean_sums), base)
                dve.tensor_scalar(neg_mean[:, bass.ds(s, 1)], means[:, 0:1], -1.0, None, ALU.mult).then_inc(centred, 1)
                dve.tensor_scalar(deviation[:], mean_var[:, :, 0], means[:, 0:1], None, ALU.subtract)
                link(dve.scalar_tensor_tensor(share_dev[:], mean_var[:, :, 0], means[:, 0:1], share_sb[:, :, 0],
                                              ALU.subtract, ALU.mult), base)
                link(dve.tensor_tensor(var_terms[:, 0:3], deviation[:], share_dev[:], ALU.mult), base)
                dve.reduce_sum(var_sum[:], var_terms[:], AX_X).then_inc(var_summed, 1)
                link(dve.reduce_sum(channel_off[:], share_dev[:], AX_X), base)
                dve.tensor_tensor(next_bias[:], out_conv_bias[:], means[:, 1:2], ALU.add).then_inc(next_bias_ready, 1)
                link(dve.tensor_scalar(fc_terms[:], fc_w_sb[:], channel_off[:, 0:1], None, ALU.mult), base)

            def scale(s):
                dve.wait_ge(variance_ready, s + 1)
                dve.tensor_scalar(var_eps[:], variance, EPS, None, ALU.add).then_inc(var_eps_ready, 1)

            def fc_input(s):
                dve.wait_ge(rstd_ready, s + 1)
                dve.scalar_tensor_tensor(fc_in[:], fc_terms[:], rstd[:, 0:1], fc_b_sb[:],
                                         ALU.mult, ALU.add).then_inc(fc_in_ready, 1)

            def softmax_input(s):
                base = STEPS * s + SETUP
                dve.wait_ge(logits_summed, s + 1)
                link(dve.reduce_max(logit_max[:], logit_sum, AX_X), base)
                dve.tensor_scalar(logits[:], logit_sum, logit_max[:, 0:1], None, ALU.subtract).then_inc(logits_ready, 1)

            def mixed_weights(s):
                base = STEPS * s + SETUP
                dve.wait_ge(exp_ready, s + 1)
                link(dve.reciprocal(inv_sum[:], exp_sum[:]), base)
                link(dve.tensor_scalar(mix[:], expd[:], inv_sum[:, 0:1], rstd[:, 0:1], ALU.mult, ALU.mult), base)
                dve.tensor_scalar(w_full[:, 0:KW:2], bands[:, 0, 0:KW:2], mix[:, 0:1], None, ALU.mult)
                link(dve.scalar_tensor_tensor(w_full[:, 1], bands[:, 0, 1], mix[:, 0:1], centre,
                                              ALU.mult, ALU.add), base)
                for e in range(1, E):
                    link(dve.scalar_tensor_tensor(w_full[:], bands[:, e], mix[:, e:e + 1], w_full[:],
                                                  ALU.mult, ALU.add), base)

            def weight_parts(s, k):
                if not isinstance(s, int) or s > 0:
                    if k < KW - 1:
                        dve.wait_ge(shift_done, (s - 1) * (KW - 1) + k + 1)
                    else:
                        dve.wait_ge(conv_done, s * TILES)
                link(dve.tensor_copy(w_hi[:, k], w_full[:, k]), STEPS * s + SETUP)
                dve.tensor_tensor(w_lo[:, k], w_full[:, k], w_hi[:, k].bitcast(F32),
                                  ALU.subtract).then_inc(weights_ready, 1)
                assert k < KW - 1 or done[0] == STEPS, done

            def stats_ahead(g, j, i, at, at_after):
                if i + AHEAD < GROUP:
                    tile_stats(g + GROUPS, j, at, i + AHEAD)
                else:
                    tile_stats(g + GROUPS + 1, j + 1, at_after, i + AHEAD - GROUP)

            def inner_turns(s, ahead):
                with dve.Fori(1, GROUPS - 1) as j:
                    g = s * GROUPS + j
                    at = ring_start(dve, g)
                    if ahead:
                        at_next = ring_start(dve, g + GROUPS, "ring_next")
                        at_after = ring_start(dve, g + GROUPS + 1, "ring_after")
                    for i in range(GROUP):
                        low(s, g * GROUP + i, at, i)
                        if ahead:
                            stats_ahead(g, j, i, at_next, at_after)

            def boundary(s, ahead=True):
                g = s * GROUPS + GROUPS - 1
                at = ring_start(dve, g)
                at_next = ring_start(dve, g + GROUPS, "ring_next")
                at_first = ring_start(dve, g + 1, "ring_first")
                if ahead:
                    at_after = ring_start(dve, g + GROUPS + 1, "ring_after")
                    at_second = ring_start(dve, g + GROUPS + 2, "ring_second")

                def first_low(i):
                    low(s + 1, (g + 1) * GROUP + i, at_first, i)

                def last_stats(i):
                    if i + AHEAD < GROUP:
                        tile_stats(g + GROUPS, GROUPS - 1, at_next, i + AHEAD)
                    elif ahead:
                        tile_stats(g + GROUPS + 1, 0, at_after, i + AHEAD - GROUP)

                def first_stats(i):
                    if ahead:
                        stats_ahead(g + 1, 0, i, at_after, at_second)

                for i in range(GROUP - AHEAD):
                    low(s, g * GROUP + i, at, i)
                    last_stats(i)
                    if i == 0:
                        early_statistics(s + 1)
                statistics(s + 1)
                low(s, g * GROUP + 3, at, 3)
                centre_and_spread(s + 1)
                low(s, g * GROUP + 4, at, 4)
                scale(s + 1)
                last_stats(3)
                fc_input(s + 1)
                last_stats(4)
                first_low(0)
                softmax_input(s + 1)
                first_stats(0)
                first_low(1)
                mixed_weights(s + 1)
                for k in range(KW):
                    weight_parts(s + 1, k)
                first_low(2)
                first_stats(1)
                first_stats(2)
                first_low(3)
                first_stats(3)
                first_low(4)
                first_stats(4)

            dve.memset(fc_b_sb[:], 0.0).then_inc(zeroed, 1)
            link(dve.memset(ones[:], 1.0))
            dve.wait_ge(bands_ready, 1)
            cols = bands[:].rearrange("p e k m -> p (e k) m")
            for j in range(ROWS):
                if j == 0:
                    place = cols[:, :, INNER:INNER + C]
                elif j == ROWS - 1:
                    place = cols[:, :, INNER + C:P]
                else:
                    place = cols[:, :, j - 1:INNER:STEP]
                dve.tensor_copy(place, band_columns(j).rearrange("p (k c) -> p k c", c=C))
            dve.wait_ge(const_loaded, 16 * 3)
            link(dve.tensor_copy(out_conv_bias[:], bias_sum))
            assert done[0] == SETUP
            dve.memset(mix[:], 0.0).then_inc(setup_done, 1)
            with dve.Fori(0, GROUPS - 1) as g:
                at = ring_start(dve, g)
                for i in range(GROUP):
                    tile_stats(g, g, at, i)
            early_statistics(0)
            for i in range(GROUP):
                tile_stats(GROUPS - 1, GROUPS - 1, (GROUPS - 1) * GROUP * W, i)
            statistics(0)
            centre_and_spread(0)
            scale(0)
            fc_input(0)
            low(0, 0, 0, 0)
            softmax_input(0)
            mixed_weights(0)
            for k in range(KW):
                weight_parts(0, k)
            for i in range(1, GROUP):
                low(0, i, 0, i)
            for i in range(AHEAD + GROUP):
                g = GROUPS + i // GROUP
                tile_stats(g, i // GROUP, (g % RING_GROUPS) * GROUP * W, i % GROUP)
            with dve.Fori(0, B - 2) as s:
                inner_turns(s, True)
                boundary(s)
            inner_turns(B - 2, True)
            boundary(B - 2, ahead=False)
            inner_turns(B - 1, False)
            last = ALL_GROUPS - 1
            for i in range(GROUP):
                low(B - 1, last * GROUP + i, (last % RING_GROUPS) * GROUP * W, i)


def kernel(x, L0_conv_w_experts, L0_conv_bias, L0_conv_fc_w, L0_conv_fc_b):
    import numpy as np
    import concourse.bacc as bacc
    from concourse.bass_utils import run_bass_kernel_spmd

    x = np.ascontiguousarray(x)
    B, C, H, W = x.shape
    E = L0_conv_w_experts.shape[0]
    expert_rows = np.ascontiguousarray(
        np.asarray(L0_conv_w_experts).transpose(3, 2, 0, 4, 1)).reshape(3 * C, E * 3 * C)

    inner = STEP * C
    c_in, r_in = np.arange(P)[:, None] // ROWS, np.arange(P)[:, None] % ROWS
    m = np.arange(P)[None, :]
    c_out = np.where(m < inner, m // STEP, (m - inner) % C)
    r_out = np.where(m < inner, m % STEP + 1, np.where(m < inner + C, 0, ROWS - 1))
    tiles = (H - 2) // STEP
    share = np.concatenate([np.where(r_in < STEP, (tiles - GROUP) / H, 0.0), np.where(r_in < STEP, GROUP / H, 0.0),
                            np.where(r_in < STEP, 0.0, 1 / H)], axis=1)
    of_group, of_out_group = (c_in // 2 == m // ROWS // 2) / 2, (c_in // 2 == c_out // 2) / 2
    identity = (c_in == c_out) & (r_in == r_out)
    constants = np.concatenate([of_group, of_out_group, identity, np.repeat(share, 2, axis=1)],
                               axis=1).astype(np.float32)
    selections = np.zeros((3, C, ROWS + 1, P), np.float32)
    for j in range(ROWS):
        for kh in range(3):
            row = j + kh - 1
            row = 1 if row < 0 else ROWS - 2 if row == ROWS else row
            for c in range(C):
                selections[kh, c, j, c * ROWS + row] = 1
    selections[0, :, ROWS] = np.arange(C)[:, None] == c_out

    arrays = {
        "x_dram": x,
        "expert_rows_dram": expert_rows,
        "bias_dram": np.ascontiguousarray(L0_conv_bias).reshape(C, 1),
        "fc_wT_dram": np.ascontiguousarray(np.asarray(L0_conv_fc_w).T),
        "fc_b_dram": np.ascontiguousarray(L0_conv_fc_b).reshape(1, E),
        "constants_dram": constants,
        "selections_dram": selections.reshape(3 * C, (ROWS + 1) * P),
    }
    nc = bacc.Bacc("TRN2", target_bir_lowering=False, num_devices=1, dynamic_dma_scratch_size=256)
    args = [nc.dram_tensor(n, a.shape, mybir.dt.from_np(a.dtype), kind="ExternalInput").ap() for n, a in arrays.items()]
    args.append(nc.dram_tensor("out_dram", x.shape, mybir.dt.from_np(x.dtype), kind="ExternalOutput").ap())
    conv_kernel(nc, *args)
    return run_bass_kernel_spmd(nc, [arrays], core_ids=[0]).results[0]["out_dram"]
```
